# Optimizing a Trainium2 kernel written in Bass

```python
import numpy as np
import jax
import jax.numpy as jnp

def _softmax(x, axis=-1):
    return jax.nn.softmax(x, axis=axis)

def _gelu(x):
    return jax.nn.gelu(x, approximate=True)

def _silu(x):
    return jax.nn.silu(x)

def _sigmoid(x):
    return jax.nn.sigmoid(x)

def _layernorm(x, axis=-1, eps=1e-05):
    m = jnp.mean(x, axis=axis, keepdims=True)
    v = jnp.var(x, axis=axis, keepdims=True)
    return (x - m) / jnp.sqrt(v + eps)

def _scatter_add(tgt, idx, src, axis=0):
    return tgt.at[idx].add(src)

def _segment_sum(src, seg, n):
    return jax.ops.segment_sum(src, seg, n)
kernel_name = 'mk_gnn_preln_d2_gnn_r32_714f70'

def setup_inputs(seed: int=0):
    np.random.seed(seed)
    _w = jnp.asarray

    def _rec_inputs():
        import jax
        import jax.numpy as jnp
        _gk = jax.random.key(seed)
        x = -0.000202 + 1 * jax.random.normal(jax.random.fold_in(_gk, 1), (3125, 128), jnp.float32)
        _s = jax.random.randint(jax.random.fold_in(_gk, 2), (25000,), 0, 3125, jnp.int32)
        _d = jax.random.randint(jax.random.fold_in(_gk, 3), (25000,), 0, 3125, jnp.int32)
        _loop = jnp.arange(3125, dtype=jnp.int32)
        src = jnp.concatenate([_s, _d, _loop])
        dst = jnp.concatenate([_d, _s, _loop])
        _o = jnp.argsort(dst, stable=True)
        src = src[_o]
        dst = dst[_o]
        return (x, src, dst)
    x, src, dst = _rec_inputs()

    def _L0_gnn_setup():
        import jax, jax.numpy as jnp
        import numpy as np
        N_NODES = 50000
        N_EDGES = 25000
        IN_DIM = 128
        HID = 128
        TIME = 6.0
        STEPS = 12
        key = jax.random.key(seed)
        ks = jax.random.split(key, 8)
        gat_out = jax.random.normal(ks[0], (N_NODES, IN_DIM), dtype=jnp.float32)
        edge_index = jax.random.randint(ks[1], (2, N_EDGES), 0, N_NODES, dtype=jnp.int64)
        W_in = jax.random.normal(ks[2], (IN_DIM, HID), dtype=jnp.float32) * (1.0 / np.sqrt(IN_DIM))
        b_in = jnp.zeros((HID,), dtype=jnp.float32)
        W1 = jax.random.normal(ks[3], (HID, 2 * HID), dtype=jnp.float32) * (1.0 / np.sqrt(HID))
        b1 = jnp.zeros((2 * HID,), dtype=jnp.float32)
        W2 = jax.random.normal(ks[4], (2 * HID, HID), dtype=jnp.float32) * (1.0 / np.sqrt(2 * HID))
        b2 = jnp.zeros((HID,), dtype=jnp.float32)
        clearance = jnp.full((1,), 0.1, dtype=jnp.float32)
        return {'gat_out': gat_out, 'edge_index': edge_index, 'W_in': W_in, 'b_in': b_in, 'W1': W1, 'b1': b1, 'W2': W2, 'b2': b2, 'clearance': clearance}
    _L0_gnn_all = _L0_gnn_setup()
    _L0_gnn_in = {k: v for k, v in _L0_gnn_all.items() if k in ('W_in', 'b_in', 'W1', 'b1', 'W2', 'b2', 'clearance')}
    del _L0_gnn_all

    def _L1_gnn_setup():
        import jax, jax.numpy as jnp
        import numpy as np
        N_NODES = 50000
        N_EDGES = 25000
        D_IN = 128
        D_HID = 128
        D_OUT = 128

        def gcn_conv(x, src, dst, W, b):
            N = x.shape[0]
            h = x @ W
            deg = jnp.zeros((N,), h.dtype).at[dst].add(jnp.ones((), h.dtype))
            dinv = jax.lax.rsqrt(deg)
            norm = dinv[src] * dinv[dst]
            msg = h[src] * norm[:, None]
            out = jax.ops.segment_sum(msg, dst, num_segments=N)
            return out + b
        key = jax.random.key(seed)
        ks = jax.random.split(key, 6)
        x = jax.random.normal(ks[0], (N_NODES, D_IN), dtype=jnp.float32)
        edge_index = jax.random.randint(ks[1], (2, N_EDGES), 0, N_NODES, dtype=jnp.int64)
        s_in = 1.0 / np.sqrt(D_IN)
        s_hid = 1.0 / np.sqrt(D_HID)
        W1 = jax.random.normal(ks[2], (D_IN, D_HID), dtype=jnp.float32) * s_in
        b1 = jnp.zeros((D_HID,), dtype=jnp.float32)
        W2 = jax.random.normal(ks[3], (D_HID, D_OUT), dtype=jnp.float32) * s_hid
        b2 = jnp.zeros((D_OUT,), dtype=jnp.float32)
        return {'x': x, 'edge_index': edge_index, 'W1': W1, 'b1': b1, 'W2': W2, 'b2': b2}
    _L1_gnn_all = _L1_gnn_setup()
    _L1_gnn_in = {k: v for k, v in _L1_gnn_all.items() if k in ('W1', 'b1', 'W2', 'b2')}
    del _L1_gnn_all
    return {'x': x, 'src': src, 'dst': dst, 'L0_gnn_W_in': _L0_gnn_in['W_in'], 'L0_gnn_b_in': _L0_gnn_in['b_in'], 'L0_gnn_W1': _L0_gnn_in['W1'], 'L0_gnn_b1': _L0_gnn_in['b1'], 'L0_gnn_W2': _L0_gnn_in['W2'], 'L0_gnn_b2': _L0_gnn_in['b2'], 'L0_gnn_clearance': _L0_gnn_in['clearance'], 'L1_gnn_W1': _L1_gnn_in['W1'], 'L1_gnn_b1': _L1_gnn_in['b1'], 'L1_gnn_W2': _L1_gnn_in['W2'], 'L1_gnn_b2': _L1_gnn_in['b2']}

def reference(x, src, dst, L0_gnn_W_in, L0_gnn_b_in, L0_gnn_W1, L0_gnn_b1, L0_gnn_W2, L0_gnn_b2, L0_gnn_clearance, L1_gnn_W1, L1_gnn_b1, L1_gnn_W2, L1_gnn_b2):
    import jax
    import jax.numpy as jnp

    def _L0_gnn_ref(gat_out, edge_index, W_in, b_in, W1, b1, W2, b2, clearance):
        import jax, jax.numpy as jnp
        import numpy as np
        N_NODES = 50000
        N_EDGES = 25000
        IN_DIM = 128
        HID = 128
        TIME = 6.0
        STEPS = 12
        N = gat_out.shape[0]
        dt = TIME / STEPS
        src, dst = (edge_index[0], edge_index[1])
        h = jnp.tanh(gat_out @ W_in + b_in)
        deg = jax.ops.segment_sum(jnp.ones((src.shape[0],), dtype=h.dtype), dst, num_segments=N)
        deg = jnp.clip(deg, 1.0, None)[:, None]
        decay = jax.nn.relu(clearance)

        def step(h, _):
            agg = jax.ops.segment_sum(h[src], dst, num_segments=N) / deg
            diff = jnp.tanh(jax.nn.gelu(agg @ W1 + b1, approximate=False) @ W2 + b2)
            h = h + (diff - decay * h) * dt
            return (h, None)
        h, _ = jax.lax.scan(step, h, None, length=STEPS)
        return h

    def _L1_gnn_ref(x, edge_index, W1, b1, W2, b2):
        import jax, jax.numpy as jnp
        import numpy as np
        N_NODES = 50000
        N_EDGES = 25000
        D_IN = 128
        D_HID = 128
        D_OUT = 128

        def gcn_conv(x, src, dst, W, b):
            N = x.shape[0]
            h = x @ W
            deg = jnp.zeros((N,), h.dtype).at[dst].add(jnp.ones((), h.dtype))
            dinv = jax.lax.rsqrt(deg)
            norm = dinv[src] * dinv[dst]
            msg = h[src] * norm[:, None]
            out = jax.ops.segment_sum(msg, dst, num_segments=N)
            return out + b
        N = x.shape[0]
        loop = jnp.arange(N, dtype=edge_index.dtype)
        src = jnp.concatenate([edge_index[0], loop])
        dst = jnp.concatenate([edge_index[1], loop])
        h = jax.nn.relu(gcn_conv(x, src, dst, W1, b1))
        out = gcn_conv(h, src, dst, W2, b2)
        return out
    edge_index = jnp.stack([src, dst])
    h = jnp.maximum(_layernorm(x, axis=-1), 0.0)
    x = x + _L0_gnn_ref(h, edge_index, L0_gnn_W_in, L0_gnn_b_in, L0_gnn_W1, L0_gnn_b1, L0_gnn_W2, L0_gnn_b2, L0_gnn_clearance)
    h = jnp.maximum(_layernorm(x, axis=-1), 0.0)
    x = x + _L1_gnn_ref(h, edge_index, L1_gnn_W1, L1_gnn_b1, L1_gnn_W2, L1_gnn_b2)
    return x

_drawn_inputs = setup_inputs


def setup_inputs(seed=0):
    import zlib

    import numpy as np

    out = dict(_drawn_inputs(seed))
    spreads = {'L0_gnn_b_in': (0.0, 0.1),
     'L0_gnn_b1': (0.0, 0.1),
     'L0_gnn_b2': (0.0, 0.1),
     'L1_gnn_b1': (0.0, 0.296),
     'L1_gnn_b2': (0.0, 0.1)}
    factors = {}
    for name, (base, spread) in spreads.items():
        noise = np.random.default_rng([zlib.crc32(name.encode()), seed]).standard_normal(out[name].shape)
        drawn = base * np.exp(spread * noise) if base else spread * noise
        out[name] = jnp.asarray(drawn.astype(out[name].dtype))
    for name, factor in factors.items():
        out[name] = (out[name] * factor).astype(out[name].dtype)
    return out
```

```python
from contextlib import ExitStack

import concourse.bass as bass
from concourse import mybir

F32 = mybir.dt.float32
F16 = mybir.dt.float16
I32 = mybir.dt.int32
ALU = mybir.AluOpType
ACT = mybir.ActivationFunctionType
AX = mybir.AxisListType

NODES = 3125
P = 125
TILES = NODES // P
EDGES = 53125
FEAT = 128
HID = 256
STEPS = 12
DT = 0.5
EPS = 1e-5

GROUP_TILES = 4
GROUPS = [(g * GROUP_TILES, min(GROUP_TILES, TILES - g * GROUP_TILES)) for g in range(7)]
NG = len(GROUPS)
TAIL = NG - 1

WIN = 5
WINDOWS = NODES // WIN
WCOLS = WINDOWS // P
SLOTS = 128
CHUNK = EDGES // P
BANK_WIN = 4
BATCH = 3 * BANK_WIN
BATCHES = WINDOWS // BATCH
BLOCK = NODES // 5
HALVES = [(0, 313), (313, BLOCK - 313)]
SUB = 5
TURNS = CHUNK // SUB

OPEN = 1

SPLIT_TOP = 14
LN_SCALE = 2.0**11


def gnn_kernel(nc, x, src, dst, W_in, b_in, W1, b1, W2, b2, clearance, G1, gb1, G2, gb2, out):
    ctx = ExitStack()
    with ctx:

        def sb(name, shape, dt):
            return ctx.enter_context(nc.sbuf_tensor(name, shape, dt))

        def sem(name):
            return ctx.enter_context(nc.semaphore(name))

        rdeg_dram = nc.dram_tensor("rdeg_scratch", (NODES,), F32).ap()
        dinv_dram = nc.dram_tensor("dinv_scratch", (NODES,), F32).ap()
        deg_dram = nc.dram_tensor("deg_scratch", (NODES,), F32).ap()
        x2_dram = nc.dram_tensor("x2_scratch", (NODES, FEAT), F32).ap()
        rest_dram = nc.dram_tensor("rest_scratch", (TILES, P, NODES), F16).ap()

        adj_flat = sb("adj", [P, TILES * NODES + 1], F16)
        adj = adj_flat[:, 0:TILES * NODES].rearrange("p (k d) -> p k d", k=TILES)
        state = sb("state", [P, TILES, FEAT], F32)
        hi = sb("hi", [P, TILES, FEAT], F16)
        lo = sb("lo", [P, TILES, FEAT], F16)
        w_in = sb("w_in", [FEAT, FEAT], F32)
        w1 = sb("w1", [FEAT, HID], F32)
        w2 = sb("w2", [FEAT, 2, FEAT], F32)
        wg = sb("wg", [FEAT, 2, FEAT], F32)
        bias = sb("bias", [P, 4, FEAT], F32)
        b1c = sb("b1c", [FEAT, 2], F32)
        ident = sb("ident", [P, P], F32)
        rest_tile = sb("rest_tile", [P, GROUP_TILES * P], F16)
        cols = sb("cols", [128, 296], F32)
        flag = sb("flag", [1, 1], I32)
        scratch = sb("scratch", [128, 5587], F32)

        at = [0]

        def col(n):
            at[0] += n
            return cols[:, at[0] - n:at[0]]

        decay = col(1)
        keep = col(1)
        bound = col(STEPS + 1)
        pow2 = col(STEPS + 1)
        scale = col(STEPS + 1)
        unscale = col(STEPS + 1)
        now_unscale = col(1)
        next_scale = col(1)
        top = col(4)
        mean_var = col(TILES * 2)
        ln_a = col(TILES)
        ln_b = col(TILES)
        dinv_col = col(TILES)
        part_max = col(8)
        deg = col(TILES)
        rdeg = col(TILES)
        root = col(TILES)
        dinv = col(TILES)
        assert at[0] <= 296

        row = scratch[:, 0:NODES]
        xload = scratch[0:P, 0:TILES * FEAT].rearrange("p (k f) -> p k f", f=FEAT)
        o = TILES * FEAT
        agg = [scratch[:, o:o + 500], scratch[:, o + 500:o + 625]]
        o += 625
        hid = [scratch[:, o:o + 1000].rearrange("p (h n) -> p h n", h=2),
               scratch[:, o + 1000:o + 1250].rearrange("p (h n) -> p h n", h=2)]
        lnt = [scratch[0:P, o:o + 512], scratch[0:P, o + 512:o + 1024]]
        o += 1250
        act_out = scratch[0:P, o:o + 512]
        stats = scratch[0:P, o:o + TILES * 6].rearrange("p (k s) -> p k s", s=6)
        ones_row = scratch[0:1, o - 225:o - 97]
        assert o + 512 == 5587
        half = scratch[:, :].bitcast(F16)
        nl, nr = 128 * BATCH, P * BATCH
        count12 = half[:, 0:nl].rearrange("p (i w) -> p i w", w=BATCH)
        o = nl
        Lb, Rb = [], []
        for _ in range(2):
            Lb.append(half[:, o:o + nl].rearrange("p (i w) -> p i w", w=BATCH))
            Rb.append(half[:, o + nl:o + nl + nr].rearrange("p (i w) -> p i w", w=BATCH))
            o += nl + nr
        src_lo = half[:, o:o + WINDOWS]
        key = half[:, o + 626:o + 626 + WINDOWS]
        o += 1252
        assert o <= 5587 * 2
        yT = [scratch[:, 768 + 500 * i:1268 + 500 * i] for i in range(2)]
        etanh = [scratch[0:P, 1768 + 512 * i:2280 + 512 * i] for i in range(2)]
        o = 0
        e_dst = scratch[0:P, o:o + CHUNK]
        e_src = scratch[0:P, o + CHUNK:o + 2 * CHUNK]
        o += 2 * CHUNK
        e_sk = scratch[0:P, o:o + CHUNK]
        e_raw = scratch[0:P, o + CHUNK:o + 2 * CHUNK]
        o += 2 * CHUNK
        h = 2 * o
        c625 = half[0:P, h:h + BLOCK]
        h += BLOCK + 1
        gL = half[0:P, h:h + SUB * 128].rearrange("p (c i) -> p c i", c=SUB)
        h += SUB * 128
        gR = half[0:P, h:h + SUB * BLOCK].rearrange("p (c i) -> p c i", c=SUB)
        h += SUB * BLOCK + 1
        g_one = half[0:P, h:h + 128]
        g_zero = half[0:P, h + 128:h + 256]
        h += 256
        g_rest = half[0:P, h:h + BLOCK]
        h += BLOCK + 1
        g_deg = scratch[0:1, h // 2:h // 2 + BLOCK]
        assert h // 2 + BLOCK <= 5587

        room = adj_flat[:, :].bitcast(F32)
        roomi = adj_flat[:, :].bitcast(I32)
        o = [0]

        def place(n, like=room):
            o[0] += n
            return like[:, o[0] - n:o[0]]

        first_i = place(1, roomi)
        first = place(1)
        thresholds = place(WINDOWS)
        below = place((WINDOWS + 1) // 2).bitcast(F16)[:, 0:WINDOWS]
        ones16 = place(64).bitcast(F16)
        wbase = place(WCOLS)
        chunk_f = place(WCOLS)
        chunk_i = place(WCOLS, roomi)
        found = place(WCOLS)
        start_f = place(WCOLS)
        start_i = place(WCOLS, roomi)
        rows_i = place(WCOLS * CHUNK, roomi).rearrange("p (g c) -> p g c", g=WCOLS)
        junk = place(WCOLS * CHUNK).rearrange("p (g c) -> p g c", g=WCOLS)
        n = WCOLS * SLOTS
        wdst_i = place(n, roomi).rearrange("p (g e) -> p g e", g=WCOLS)
        wsrc_i = place(n, roomi).rearrange("p (g e) -> p g e", g=WCOLS)
        wdst = place(n).rearrange("p (g e) -> p g e", g=WCOLS)
        wsrc = place(n)
        quot_i = place(n, roomi)
        quot = place(n)
        rem = place(n)
        over = place(n)
        inside = place(n)
        keyf = place(n)
        hits = place(n * WIN).rearrange("p (g d e) -> p g d e", g=WCOLS, d=WIN)
        deg_sum = place(1)
        ones_f = place(128)
        total = place(1)
        assert o[0] <= TILES * NODES // 2

        ps = ctx.enter_context(nc.psum_tensor("ps", [128, 8, 512], F32))
        ps_agg = [ps[:, 0, :], ps[:, 1, :], ps[:, 2, :]]
        ps_hid = [ps[:, 3, :], ps[:, 4, :]]
        ps_out = [ps[:, 5, :], ps[:, 6, :]]

        s_x = [sem(f"x_loaded{g}") for g in range(NG)]
        s_w = sem("weights_loaded")
        s_first = sem("chunk_firsts_loaded")
        s_const = sem("constants_made")
        s_below = sem("compares_made")
        s_chunk = sem("chunks_counted")
        s_chunk_i = sem("chunk_numbers_ready")
        s_rows = [sem(f"chunk_rows_loaded{g}") for g in range(WCOLS)]
        s_start = sem("window_starts_ready")
        s_wedges = sem("window_edges_loaded")
        s_keys = sem("window_keys_ready")
        s_keysT = sem("window_keys_transposed")
        s_wd = sem("window_destinations_ready")
        s_hits = sem("window_hits_ready")
        s_deg = sem("degrees_counted")
        s_degsum = sem("degrees_summed")
        s_flag = sem("flag_ready")
        s_deg1 = sem("degrees_with_loops")
        s_sqrt = sem("degree_roots_ready")
        s_norms = sem("degree_norms_ready")
        s_norms_out = sem("degree_norms_stored")
        s_norms_in = sem("inverse_degrees_loaded")
        s_var = sem("variances_ready")
        s_std = sem("deviations_ready")
        s_y = sem("entry_rows_ready")
        s_yT = sem("entry_rows_transposed")
        s_yTc = sem("entry_columns_copied")
        s_e = sem("entry_products_ready")
        s_eb = sem("entry_biased")
        s_et = sem("entry_tanh_ready")
        s_v = sem("vector_chain")
        s_kc = sem("window_keys_copied")
        s_tab = sem("scale_tables_ready")
        s_lr = [sem(f"one_hots_ready{u}") for u in range(2)]
        s_mm = [sem(f"windows_multiplied{u}") for u in range(2)]
        s_ev = [sem(f"windows_stored{u}") for u in range(2)]
        s_last = [sem(f"last_window_{n}") for n in ("one_hots", "multiplied", "stored")]
        s_now = sem("step_scales_ready")
        s_hi = sem("hi_ready")
        s_lo = sem("lo_ready")
        s_agg = sem("sums_over_edges_ready")
        s_aggT = sem("means_ready")
        s_hid = sem("hidden_products_ready")
        s_gelu = sem("gelu_ready")
        s_out = sem("step_products_ready")
        s_bias = sem("step_biased")
        s_tanh = sem("step_tanh_ready")
        s_upd = sem("state_updated")
        s_rest = [sem(f"rest_loaded{g}") for g in range(NG)]
        s_restu = sem("rest_used")
        g_in = sem("general_edges_loaded")
        g_count = sem("general_count_made")
        g_conv = sem("general_chain")
        g_ready = sem("general_one_hots_ready")
        g_done = sem("general_turn_multiplied")
        g_tile = sem("general_tile_summed")
        g_restk = sem("general_rest_kept")
        g_kept = sem("general_tile_kept")
        g_store = sem("general_rest_stored")
        g_degk = sem("general_degrees_kept")
        g_degs = sem("general_degrees_stored")
        g_degl = sem("general_degrees_loaded")
        s_xr = [sem(f"x_reloaded{g}") for g in range(NG)]
        s_x2 = sem("x2_ready")
        s_x2v = sem("x2_variances_ready")
        s_x2s = sem("x2_deviations_ready")
        s_x2o = sem("x2_stored")
        s_x2i = sem("x2_reloaded")
        s_dinv = sem("dinv_row_loaded")
        c_hi = sem("gcn1_hi_ready")
        c_lo = [sem(f"gcn{n}_split_ready") for n in range(2)]
        c_agg = [sem(f"gcn{n}_sums_ready") for n in range(2)]
        c_aggT = [sem(f"gcn{n}_sums_scaled") for n in range(2)]
        c_out = [sem(f"gcn{n}_products_ready") for n in range(2)]
        c_use = [sem(f"gcn{n}_rows_ready") for n in range(2)]
        s_diag = sem("loops_added")
        s_mx = sem("maximum_reduced")
        s_mxT = sem("maximum_moved")
        s_top = sem("second_scale_ready")
        s_res = sem("result_stored")

        block = ctx.enter_context(nc.Block())
        x_v = x.rearrange("(k p) f -> p k f", p=P)
        out_v = out.rearrange("(k p) f -> p k f", p=P)
        x2_v = x2_dram.rearrange("(k p) f -> p k f", p=P)

        def tiles_of(t, g):
            k0, nt = GROUPS[g]
            return t[:, k0:k0 + nt, :].rearrange("p k f -> p (k f)")

        def window_layout(a):
            return a.rearrange("(g q d) -> q g d", g=WCOLS, q=P)

        @block.sync
        def _(sp):
            for done in (g_store, g_degs):
                sp.sem_inc(done, 16 * OPEN)
            with nc.allow_non_contiguous_dma("125 single integers"):
                sp.dma_start(first_i, dst.rearrange("(p c) -> p c", c=CHUNK)[:, 0:1]).then_inc(s_first, 16)
            for g in range(NG):
                k0, nt = GROUPS[g]
                sp.dma_start(state[:, k0:k0 + nt, :], x_v[:, k0:k0 + nt, :]).then_inc(s_x[g], 16)
            sp.dma_start(w_in[:, :], W_in).then_inc(s_w, 16)
            sp.dma_start(w1[:, :], W1).then_inc(s_w, 16)
            sp.dma_start(w2[:, :, :], W2.rearrange("(h p) f -> p h f", p=FEAT)).then_inc(s_w, 16)
            sp.dma_start(wg[:, 0, :], G1).then_inc(s_w, 16)
            sp.dma_start(wg[:, 1, :], G2).then_inc(s_w, 16)
            for i, b in enumerate((b_in, b2, gb1, gb2)):
                sp.dma_start(bias[:, i, :], b.rearrange("(a f) -> a f", a=1).broadcast_to((P, FEAT))
                             ).then_inc(s_w, 16)
            with nc.allow_non_contiguous_dma("a bias of 256 as two columns"):
                sp.dma_start(b1c[:, :], b1.rearrange("(h p) -> p h", p=FEAT)).then_inc(s_w, 16)
            with nc.allow_non_contiguous_dma("one float on every partition"):
                sp.dma_start(decay, clearance.rearrange("(a f) -> a f", a=1).broadcast_to((128, 1))
                             ).then_inc(s_w, 16)

            sp.wait_ge(s_flag, 1)
            missed = sp.value_load(flag[0:1, 0:1], min_val=0, max_val=1)
            with sp.If(missed != 0):
                sp.wait_ge(s_last[2], 1)
                sp.dma_start(e_raw.bitcast(I32), dst.rearrange("(p c) -> p c", c=CHUNK)).then_inc(g_in, 16)
                sp.dma_start(e_sk.bitcast(I32), src.rearrange("(p c) -> p c", c=CHUNK)).then_inc(g_in, 16)
                with sp.Fori(0, 5) as j:
                    with sp.Fori(0, TILES) as k:
                        sp.wait_ge(g_kept, j * TILES + k + 1 + OPEN)
                        sp.dma_start(rest_dram[bass.ds(k, 1), :, bass.ds(j * BLOCK, BLOCK)].rearrange("k p d -> p (k d)"),
                                     g_rest).then_inc(g_store, 16)
                    sp.wait_ge(g_degk, j + 1 + OPEN)
                    sp.dma_start(deg_dram[bass.ds(j * BLOCK, BLOCK)].rearrange("(a n) -> a n", a=1),
                                 g_deg).then_inc(g_degs, 16)
                sp.wait_ge(g_store, 16 * (5 * TILES + OPEN))
                sp.wait_ge(g_degs, 16 * (5 + OPEN))
                sp.dma_start(deg[0:P, :].rearrange("p (g d) -> p g d", g=WCOLS), window_layout(deg_dram)
                             ).then_inc(g_degl, 16)

            sp.wait_ge(s_norms, 1)
            sp.dma_start(window_layout(rdeg_dram), rdeg[0:P, :].rearrange("p (g d) -> p g d", g=WCOLS)
                         ).then_inc(s_norms_out, 16)
            sp.dma_start(window_layout(dinv_dram), dinv[0:P, :].rearrange("p (g d) -> p g d", g=WCOLS)
                         ).then_inc(s_norms_out, 16)
            sp.wait_ge(s_norms_out, 32)
            sp.wait_ge(s_last[2], 1)
            sp.dma_start(row, rdeg_dram.rearrange("(a n) -> a n", a=1).broadcast_to((128, NODES))
                         ).then_inc(s_norms_in, 16)
            with nc.allow_non_contiguous_dma("a column of one float per node"):
                sp.dma_start(dinv_col[0:P, :], dinv_dram.rearrange("(k p) -> p k", p=P)).then_inc(s_norms_in, 16)

            def stream_rest(turn, g):
                k0, nt = GROUPS[g]
                with sp.Fori(0, TILES) as k:
                    sp.wait_ge(s_restu, (turn * NG + g) * TILES + k + OPEN)
                    sp.dma_start(rest_tile[:, 0:nt * P],
                                 rest_dram[bass.ds(k, 1), :, k0 * P:(k0 + nt) * P].rearrange("k p d -> p (k d)")
                                 ).then_inc(s_rest[g], 16)

            with sp.If(missed != 0):
                with sp.Fori(0, STEPS) as t:
                    for g in range(NG):
                        stream_rest(t, g)

            sp.wait_ge(s_aggT, NG * STEPS + OPEN)
            for g in range(NG):
                k0, nt = GROUPS[g]
                sp.dma_start(xload[:, k0:k0 + nt, :], x_v[:, k0:k0 + nt, :]).then_inc(s_xr[g], 16)
            sp.wait_ge(s_x2, NG)
            sp.dma_start(row, dinv_dram.rearrange("(a n) -> a n", a=1).broadcast_to((128, NODES))
                         ).then_inc(s_dinv, 16)
            sp.dma_start(x2_v, state[:, :, :]).then_inc(s_x2o, 16)
            with sp.If(missed != 0):
                for g in range(NG):
                    stream_rest(STEPS, g)
            sp.wait_ge(s_x2o, 16)
            sp.wait_ge(c_lo[1], NG)
            sp.dma_start(state[:, :, :], x2_v).then_inc(s_x2i, 16)
            with sp.If(missed != 0):
                for g in range(NG):
                    stream_rest(STEPS + 1, g)
            for g in range(NG):
                k0, nt = GROUPS[g]
                sp.wait_ge(c_use[1], g + 1)
                sp.dma_start(out_v[:, k0:k0 + nt, :], state[:, k0:k0 + nt, :]).then_inc(s_res, 16)
            sp.wait_ge(s_res, 16 * NG)

        @block.gpsimd
        def _(pool):
            big = dict(allow_small_or_imprecise_dtypes=True)
            nc.gpsimd.iota(thresholds, pattern=[[WIN, WINDOWS]], base=0, channel_multiplier=0, **big)
            nc.gpsimd.iota(wbase, pattern=[[P * WIN, WCOLS]], base=0, channel_multiplier=WIN, **big)
            nc.gpsimd.memset(ones_f, 1.0)
            nc.gpsimd.memset(ones16, 1.0).then_inc(s_const, 1)
            nc.gpsimd.memset(ident[:, :], 0.0).then_inc(s_const, 1)
            pool.wait_ge(s_const, 2)
            nc.gpsimd.affine_select(out=ident[:, :], in_=ident[:, :], compare_op=ALU.not_equal, fill=1.0,
                                    base=0, pattern=[[-1, P]], channel_multiplier=1)
            nc.gpsimd.iota(count12, pattern=[[1, 128], [0, BATCH]], base=0, channel_multiplier=0, **big
                           ).then_inc(s_const, 1)
            pool.wait_ge(s_chunk_i, 1)
            for g in range(WCOLS):
                nc.gpsimd.indirect_dma_start(
                    rows_i[:, g, :], None, dst.rearrange("(n o) -> n o", o=1),
                    bass.IndirectOffsetOnAxis(ap=chunk_i[:, g:g + 1], axis=0)).then_inc(s_rows[g], 16)
            pool.wait_ge(s_start, 1)
            for g in range(WCOLS):
                for rows, edges in ((wdst_i, dst), (wsrc_i, src)):
                    nc.gpsimd.indirect_dma_start(
                        rows[:, g, :], None, edges.rearrange("(n o) -> n o", o=1),
                        bass.IndirectOffsetOnAxis(ap=start_i[:, g:g + 1], axis=0)).then_inc(s_wedges, 16)
            pool.wait_ge(s_wd, 1)
            for d in range(WIN):
                last = nc.gpsimd.tensor_scalar(hits[:, :, d, :], wdst, float(d), None, ALU.is_equal)
            last.then_inc(s_hits, 1)
            pool.wait_ge(s_flag, 1)
            missed = pool.value_load(flag[0:1, 0:1], min_val=0, max_val=1)
            with pool.If(missed != 0):
                pool.wait_ge(s_last[2], 1)
                nc.gpsimd.iota(c625, pattern=[[1, BLOCK]], base=0, channel_multiplier=0, **big).then_inc(g_count, 1)

        @block.tensor
        def _(pe):
            for done in (*s_mm, g_done, s_restu, s_hid, s_out):
                pe.sem_inc(done, OPEN)
            pe.wait_ge(s_below, 1)
            for g in range(WCOLS):
                mm = nc.tensor.matmul(ps[0:P, 7, g:g + 1], below[:, g * P:(g + 1) * P], ones16[:, 0:1],
                                      start=True, stop=True)
            mm.then_inc(s_chunk, 1)

            def entry_transpose(g):
                k0, nt = GROUPS[g]
                pe.wait_ge(s_y, g + 1)
                if g >= 2:
                    pe.wait_ge(s_yTc, g - 1)
                for i in range(nt):
                    mm = nc.tensor.transpose(ps[:, g % 2, i * P:(i + 1) * P], state[:, k0 + i, :], ident[:, :])
                mm.then_inc(s_yT, 1)

            def entry_product(g):
                k0, nt = GROUPS[g]
                pe.wait_ge(s_yTc, g + 1)
                if g >= 2:
                    pe.wait_ge(s_et, g - 1)
                for i in range(nt):
                    mm = nc.tensor.matmul(ps[0:P, 2 + g % 2, i * FEAT:(i + 1) * FEAT],
                                          yT[g % 2][:, i * P:(i + 1) * P], w_in[:, :], start=True, stop=True)
                mm.then_inc(s_e, 1)

            pe.wait_ge(s_const, 3)
            pe.wait_ge(s_w, 16 * 11)
            entry_transpose(0)
            for g in range(NG):
                if g + 1 < NG:
                    entry_transpose(g + 1)
                entry_product(g)

            pe.wait_ge(s_keys, 1)
            pe.wait_ge(s_et, NG)
            for n, t in enumerate((rem, keyf)):
                for g in range(WCOLS):
                    mm = nc.tensor.transpose(ps[:, 2 * n + g // 4, (g % 4) * P:(g % 4 + 1) * P],
                                             t[:, g * SLOTS:(g + 1) * SLOTS], ident[:, :])
            mm.then_inc(s_keysT, 1)
            pe.wait_ge(s_deg, 1)
            nc.tensor.matmul(ps[0:P, 7, 8:9], ones_f[:, 0:P], deg_sum, start=True, stop=True).then_inc(s_degsum, 1)
            pe.wait_ge(s_kc, 1)

            def window(buf, w, bank, place):
                target = bank[:, 0:TILES * BANK_WIN * WIN].rearrange("p (k c) -> p k c", k=TILES)
                return nc.tensor.matmul(target[:, :, place * WIN:(place + 1) * WIN], Lb[buf][:, :, w],
                                        Rb[buf][:, :, w].rearrange("p (k d) -> p k d", d=WIN),
                                        start=True, stop=True)

            with pe.Fori(0, BATCHES // 2) as i:
                for u in range(2):
                    pe.wait_ge(s_lr[u], i + 1)
                    pe.wait_ge(s_ev[u], i + OPEN)
                    for w in range(BATCH):
                        mm = window(u, w, ps[:, 3 * u + w // BANK_WIN, :], w % BANK_WIN)
                    mm.then_inc(s_mm[u], 1)
            pe.wait_ge(s_last[0], 1)
            window(0, 0, ps[:, 6, :], 0).then_inc(s_last[1], 1)

            missed = pe.value_load(flag[0:1, 0:1], min_val=0, max_val=1)
            with pe.If(missed != 0):
                pe.wait_ge(s_last[2], 1)
                pe.wait_ge(g_conv, 1)

                def tile_sum(j, number, left):
                    first = (j * (TILES + 1) + number) * TURNS
                    pe.wait_ge(g_ready, first + 1)
                    for b, (c0, n) in enumerate(HALVES):
                        nc.tensor.matmul(ps[:, b, 0:n], g_zero, c625[:, c0:c0 + n], start=True, stop=False)
                    with pe.Fori(0, TURNS) as c:
                        pe.wait_ge(g_ready, first + c + 1)
                        for s in range(SUB):
                            for b, (c0, n) in enumerate(HALVES):
                                mm = nc.tensor.matmul(ps[:, b, 0:n], left(s), gR[:, s, c0:c0 + n],
                                                      start=False, stop=False)
                        mm.then_inc(g_done, 1)
                    for b, (c0, n) in enumerate(HALVES):
                        mm = nc.tensor.matmul(ps[:, b, 0:n], g_zero, c625[:, c0:c0 + n], start=False, stop=True)
                    mm.then_inc(g_tile, 1)

                with pe.Fori(0, 5) as j:
                    with pe.Fori(0, TILES) as k:
                        pe.wait_ge(g_kept, j * TILES + k + OPEN)
                        pe.wait_ge(g_degk, j + OPEN)
                        tile_sum(j, k, lambda s: gL[:, s, :])
                    pe.wait_ge(g_kept, j * TILES + TILES + OPEN)
                    tile_sum(j, TILES, lambda s: g_one)
                pe.wait_ge(g_degk, 5 + OPEN)

            def edge_sums(turn, g, split, first):
                k0, nt = GROUPS[g]
                c0, n = k0 * P, nt * P
                bank = ps_agg[2 if g == TAIL else g % 2][:, 0:n]
                for k in range(TILES):
                    if g == 0 and k % GROUP_TILES == 0:
                        pe.wait_ge(split, first + k // GROUP_TILES + 1)
                    if k == TILES - 1:
                        with pe.If(missed != 0):
                            with pe.Fori(0, TILES) as r:
                                pe.wait_ge(s_rest[g], (turn * TILES + r + 1) * 16)
                                nc.tensor.matmul(bank, hi[:, bass.ds(r, 1), :].rearrange("p k f -> p (k f)"),
                                                 rest_tile[:, 0:n], start=False, stop=False)
                                nc.tensor.matmul(bank, lo[:, bass.ds(r, 1), :].rearrange("p k f -> p (k f)"),
                                                 rest_tile[:, 0:n], start=False, stop=False).then_inc(s_restu, 1)
                    nc.tensor.matmul(bank, hi[:, k, :], adj[:, k, c0:c0 + n], start=(k == 0), stop=False)
                    mm = nc.tensor.matmul(bank, lo[:, k, :], adj[:, k, c0:c0 + n], start=False,
                                          stop=(k == TILES - 1))
                return mm

            pe.wait_ge(s_last[2], 1)
            with pe.Fori(0, STEPS) as t:
                def hidden(g):
                    n = GROUPS[g][1] * P
                    pe.wait_ge(s_aggT, t * NG + g + 1 + OPEN)
                    pe.wait_ge(s_gelu, t * 2 * NG + 2 * g + OPEN)
                    for h in range(2):
                        nc.tensor.matmul(ps_hid[h][:, 0:n], w1[:, h * FEAT:(h + 1) * FEAT],
                                         agg[g == TAIL][:, 0:n], start=True, stop=True).then_inc(s_hid, 1)

                def outputs(g):
                    nt = GROUPS[g][1]
                    pe.wait_ge(s_gelu, t * 2 * NG + 2 * g + 2 + OPEN)
                    pe.wait_ge(s_tanh, t * NG + (g if g < TAIL else 0) + OPEN)
                    for i in range(nt):
                        for h in range(2):
                            mm = nc.tensor.matmul(ps_out[g == TAIL][0:P, i * FEAT:(i + 1) * FEAT],
                                                  hid[g == TAIL][:, h, i * P:(i + 1) * P], w2[:, h, :],
                                                  start=(h == 0), stop=(h == 1))
                    mm.then_inc(s_out, 1)

                for g in range(NG):
                    pe.wait_ge(s_aggT, t * NG + max(g - 1, 0) + OPEN)
                    edge_sums(t, g, s_lo, t * NG).then_inc(s_agg, 1)
                    if g >= 2:
                        outputs(g - 2)
                    if g >= 1:
                        hidden(g - 1)
                hidden(TAIL)
                outputs(TAIL - 1)
                outputs(TAIL)

            pe.wait_ge(s_diag, 1)
            for layer in range(2):
                def product(g):
                    nt = GROUPS[g][1]
                    pe.wait_ge(c_aggT[layer], g + 1)
                    if 0 < g < TAIL:
                        pe.wait_ge(c_use[layer], g)
                    for i in range(nt):
                        mm = nc.tensor.matmul(ps_out[g == TAIL][0:P, i * FEAT:(i + 1) * FEAT],
                                              agg[g == TAIL][:, i * P:(i + 1) * P], wg[:, layer, :],
                                              start=True, stop=True)
                    mm.then_inc(c_out[layer], 1)

                for g in range(NG):
                    if 2 <= g < TAIL:
                        pe.wait_ge(c_aggT[layer], g - 1)
                    edge_sums(STEPS + layer, g, c_lo[layer], 0).then_inc(c_agg[layer], 1)
                    if g >= 1:
                        product(g - 1)
                product(TAIL)
                if layer == 0:
                    pe.wait_ge(s_mx, 1)
                    nc.tensor.transpose(ps[0:1, 7, 0:P], part_max[0:P, 7:8], ident[:, :]).then_inc(s_mxT, 1)
                    pe.wait_ge(s_mx, 2)
                    nc.tensor.matmul(ps[:, 7, 128:129], ones_row, top[0:1, 0:1], start=True, stop=True
                                     ).then_inc(s_mxT, 1)

        @block.scalar
        def _(act):
            def split_hi(group, state_count, factor):
                act.wait_ge(s_upd, state_count)
                nc.scalar.activation(tiles_of(hi, group), tiles_of(state, group), ACT.Copy, scale=factor
                                     ).then_inc(s_hi, 1)

            for done in (*s_ev, s_gelu, s_tanh):
                act.sem_inc(done, OPEN)
            act.wait_ge(s_var, 1)
            nc.scalar.activation(ln_a[0:P, :], ln_b[0:P, :], ACT.Sqrt).then_inc(s_std, 1)
            act.wait_ge(s_tab, 1)
            for g in range(NG):
                n = GROUPS[g][1] * FEAT
                act.wait_ge(s_eb, g + 1)
                if g >= 2:
                    act.wait_ge(s_upd, g - 1)
                nc.scalar.activation(etanh[g % 2][:, 0:n], ps[0:P, 2 + g % 2, 0:n], ACT.Tanh).then_inc(s_et, 1)
                if g >= 1:
                    split_hi(g - 1, g, scale[0:P, 0:1])
            split_hi(TAIL, NG, scale[0:P, 0:1])

            with act.Fori(0, BATCHES // 2) as i:
                for u in range(2):
                    act.wait_ge(s_mm[u], i + 1 + OPEN)
                    act.wait_ge(s_kc, 1)
                    nc.scalar.activation(
                        adj[:, :, bass.ds((i * 2 + u) * BATCH * WIN, BATCH * WIN)].rearrange(
                            "p k (b c) -> p b k c", b=3),
                        ps[0:P, 3 * u:3 * u + 3, 0:TILES * BANK_WIN * WIN].rearrange(
                            "p b (k c) -> p b k c", k=TILES), ACT.Copy).then_inc(s_ev[u], 1)
            act.wait_ge(s_last[1], 1)
            nc.scalar.activation(
                adj[:, :, NODES - WIN:NODES],
                ps[0:P, 6, 0:TILES * BANK_WIN * WIN].rearrange("p (k c) -> p k c", k=TILES)[:, :, 0:WIN],
                ACT.Copy).then_inc(s_last[2], 1)

            act.wait_ge(s_deg1, 1)
            nc.scalar.activation(root[0:P, :], root[0:P, :], ACT.Sqrt).then_inc(s_sqrt, 1)

            with act.Fori(0, STEPS) as t:
                def gelu(g):
                    n = GROUPS[g][1] * P
                    act.wait_ge(s_out, t * NG + (g if g < TAIL else 0) + OPEN)
                    for h in range(2):
                        act.wait_ge(s_hid, t * 2 * NG + 2 * g + h + 1 + OPEN)
                        nc.scalar.activation(hid[g == TAIL][:, h, 0:n], ps_hid[h][:, 0:n], ACT.Gelu,
                                             bias=b1c[:, h:h + 1], scale=now_unscale
                                             ).then_inc(s_gelu, 1)

                def tanh(g):
                    n = GROUPS[g][1] * FEAT
                    act.wait_ge(s_bias, t * NG + g + 1)
                    act.wait_ge(s_upd, (t + 1) * NG + g)
                    nc.scalar.activation(act_out[:, 0:n], ps_out[g == TAIL][0:P, 0:n], ACT.Tanh
                                         ).then_inc(s_tanh, 1)

                def next_hi(g):
                    split_hi(g, (t + 1) * NG + g + 1, next_scale[0:P, :])

                act.wait_ge(s_now, t + 1)
                for g in range(1, NG):
                    if g >= 2:
                        tanh(g - 2)
                    gelu(g - 1)
                gelu(TAIL)
                act.wait_ge(s_agg, (t + 1) * NG)
                for g in range(3):
                    next_hi(g)
                tanh(TAIL - 1)
                for g in range(3, TAIL - 1):
                    next_hi(g)
                tanh(TAIL)
                for g in range(TAIL - 1, NG):
                    next_hi(g)

            act.wait_ge(s_x2v, 1)
            nc.scalar.activation(ln_a[0:P, :], ln_b[0:P, :], ACT.Sqrt).then_inc(s_x2s, 1)
            act.wait_ge(s_top, 1)
            act.wait_ge(c_agg[0], NG)
            for g in range(NG):
                nc.scalar.activation(tiles_of(hi, g), tiles_of(state, g), ACT.Copy, scale=top[0:P, 2:3]
                                     ).then_inc(c_hi, 1)

        @block.vector
        def _(dve):
            chain = [0]

            def link(ins):
                chain[0] += 1
                ins.then_inc(s_v, 1)
                dve.wait_ge(s_v, chain[0])

            V = nc.vector
            for done in (g_kept, g_degk, s_aggT):
                dve.sem_inc(done, OPEN)

            dve.wait_ge(s_first, 16)
            dve.wait_ge(s_const, 3)
            link(V.tensor_copy(first, first_i))
            V.tensor_scalar(below, thresholds, first, None, ALU.is_gt).then_inc(s_below, 1)
            dve.wait_ge(s_chunk, 1)
            link(V.tensor_scalar(chunk_f, ps[0:P, 7, 0:WCOLS], -1.0, 0.0, ALU.add, ALU.max))
            link(V.tensor_scalar(chunk_f, chunk_f, float(CHUNK), None, ALU.mult))
            V.tensor_copy(chunk_i, chunk_f).then_inc(s_chunk_i, 1)

            dve.wait_ge(s_w, 16 * 11)
            link(V.tensor_scalar(keep, decay, 0.0, -DT, ALU.max, ALU.mult))
            link(V.tensor_scalar(keep, keep, 1.0, None, ALU.add))
            link(V.scalar_tensor_tensor(out=decay, in0=keep, scalar=-1.0, in1=keep, op0=ALU.mult, op1=ALU.max))
            link(V.memset(bound[:, 0:1], 2.0))
            for t in range(STEPS):
                link(V.tensor_scalar(bound[:, t + 1:t + 2], bound[:, t:t + 1], decay, 1.0 / (2 * DT),
                                     ALU.mult, ALU.add))

            def power_of_two(dst_, inverse, src_):
                link(V.tensor_scalar(dst_.bitcast(I32), src_.bitcast(I32), 0x7F800000, None, ALU.bitwise_and))
                link(V.tensor_scalar(inverse.bitcast(I32), dst_.bitcast(I32), -1.0, float(254 << 23),
                                     ALU.mult, ALU.add))

            power_of_two(pow2, scale, bound)
            link(V.tensor_scalar(scale, scale, 2.0**SPLIT_TOP, None, ALU.mult))
            V.tensor_scalar(unscale, pow2, 2.0**-SPLIT_TOP * DT, None, ALU.mult).then_inc(s_tab, 1)

            mv = mean_var[0:P, :].rearrange("p (k s) -> p k s", s=2)

            def statistics(rows):
                for k in range(TILES):
                    if k % GROUP_TILES == 0:
                        rows(k // GROUP_TILES)
                    last = V.bn_stats(stats[:, k, :], state[:, k, :])
                link(last)
                for k in range(TILES):
                    last = V.bn_aggr(mv[:, k, :], stats[:, k, :])
                link(last)
                return V.tensor_scalar(ln_b[0:P, :], mv[:, :, 1], EPS, None, ALU.add)

            for g in range(WCOLS):
                dve.wait_ge(s_rows[g], 16)
                last = V.tensor_scalar(junk[:, g, :], rows_i[:, g, :], wbase[:, g:g + 1], 0.0, ALU.is_lt, ALU.add,
                                       accum_out=found[:, g:g + 1])
            link(last)
            link(V.tensor_tensor(start_f, found, chunk_f, ALU.add))
            link(V.tensor_scalar(start_f, start_f, float(EDGES - SLOTS), None, ALU.min))
            V.tensor_copy(start_i, start_f).then_inc(s_start, 1)

            statistics(lambda g: dve.wait_ge(s_x[g], 16)).then_inc(s_var, 1)
            dve.wait_ge(s_std, 1)
            link(V.reciprocal(ln_a[0:P, :], ln_a[0:P, :]))
            link(V.scalar_tensor_tensor(out=ln_b[0:P, :], in0=mv[:, :, 0], scalar=-1.0, in1=ln_a[0:P, :],
                                        op0=ALU.mult, op1=ALU.mult))
            for g, (k0, nt) in enumerate(GROUPS):
                for k in range(k0, k0 + nt):
                    last = V.tensor_scalar(state[:, k, :], state[:, k, :], ln_a[0:P, k:k + 1], ln_b[0:P, k:k + 1],
                                           ALU.mult, ALU.add)
                last.then_inc(s_y, 1)

            def split_lo(group, hi_count, factor):
                dve.wait_ge(s_hi, hi_count)
                V.scalar_tensor_tensor(out=tiles_of(lo, group), in0=tiles_of(state, group), scalar=factor,
                                       in1=tiles_of(hi, group), op0=ALU.mult, op1=ALU.subtract).then_inc(s_lo, 1)

            def bias_of(row_, nt):
                return bias[:, row_:row_ + 1, :].broadcast_to((P, nt, FEAT))

            def entry_copy(g):
                n = GROUPS[g][1] * P
                dve.wait_ge(s_yT, g + 1)
                if g >= 2:
                    dve.wait_ge(s_e, g - 1)
                V.tensor_scalar(yT[g % 2][:, 0:n], ps[:, g % 2, 0:n], 0.0, None, ALU.max).then_inc(s_yTc, 1)

            def entry_bias(g):
                nt = GROUPS[g][1]
                dve.wait_ge(s_e, g + 1)
                p_ = ps[0:P, 2 + g % 2, 0:nt * FEAT].rearrange("p (k f) -> p k f", f=FEAT)
                V.tensor_tensor(p_, p_, bias_of(0, nt), ALU.add).then_inc(s_eb, 1)

            def entry_state(g):
                n = GROUPS[g][1] * FEAT
                dve.wait_ge(s_et, g + 1)
                V.tensor_scalar(tiles_of(state, g), etanh[g % 2][:, 0:n], 1 / DT, None, ALU.mult).then_inc(s_upd, 1)

            entry_copy(0)
            for g in range(NG):
                if g + 1 < NG:
                    entry_copy(g + 1)
                entry_bias(g)
                if g >= 1:
                    entry_state(g - 1)
                if g >= 2:
                    split_lo(g - 2, g - 1, scale[0:P, 0:1])
            entry_state(TAIL)
            split_lo(TAIL - 1, TAIL, scale[0:P, 0:1])
            split_lo(TAIL, NG, scale[0:P, 0:1])

            n = WCOLS * SLOTS
            dve.wait_ge(s_wedges, 16 * 2 * WCOLS)
            flat = "p g e -> p (g e)"
            base = wbase.rearrange("p (g o) -> p g o", o=1).broadcast_to((P, WCOLS, SLOTS))
            V.tensor_copy(wsrc, wsrc_i.rearrange(flat))
            V.tensor_tensor(wdst, wdst_i, base, ALU.subtract).then_inc(s_wd, 1)
            dve.wait_ge(s_wd, 1)
            w_ = wdst.rearrange(flat)
            link(V.tensor_scalar(over, wsrc, 0.5 - P / 2, 1.0 / P, ALU.add, ALU.mult))
            link(V.tensor_copy(quot_i, over))
            link(V.tensor_copy(quot, quot_i))
            link(V.scalar_tensor_tensor(out=rem, in0=quot, scalar=-float(P), in1=wsrc, op0=ALU.mult, op1=ALU.add))
            link(V.tensor_scalar(over, rem, float(P), None, ALU.is_ge))
            link(V.tensor_tensor(quot, quot, over, ALU.add))
            link(V.scalar_tensor_tensor(out=rem, in0=over, scalar=-float(P), in1=rem, op0=ALU.mult, op1=ALU.add))
            V.tensor_scalar(over, w_, 0.0, None, ALU.is_ge)
            link(V.scalar_tensor_tensor(out=keyf, in0=quot, scalar=float(WIN), in1=w_, op0=ALU.mult, op1=ALU.add))
            link(V.scalar_tensor_tensor(out=inside, in0=w_, scalar=float(WIN), in1=over, op0=ALU.is_lt, op1=ALU.mult))
            link(V.scalar_tensor_tensor(out=keyf, in0=keyf, scalar=1.0, in1=inside, op0=ALU.add, op1=ALU.mult))
            V.tensor_scalar(keyf, keyf, -1.0, None, ALU.add).then_inc(s_keys, 1)
            dve.wait_ge(s_hits, 1)
            link(V.tensor_reduce(deg[0:P, :].rearrange("p (g d) -> p g d", g=WCOLS), hits, AX.X, ALU.add))
            V.tensor_reduce(deg_sum, deg[0:P, :], AX.X, ALU.add).then_inc(s_deg, 1)
            dve.wait_ge(s_degsum, 1)
            link(V.tensor_copy(total, ps[0:P, 7, 8:9]))
            V.tensor_scalar(flag[0:1, 0:1], total[0:1, :], float(EDGES), None, ALU.not_equal).then_inc(s_flag, 1)
            dve.wait_ge(s_keysT, 1)
            for n_, t_ in enumerate((src_lo, key)):
                V.tensor_copy(t_[:, 0:4 * P], ps[:, 2 * n_, 0:4 * P])
                last = V.tensor_copy(t_[:, 4 * P:5 * P], ps[:, 2 * n_ + 1, 0:P])
            last.then_inc(s_kc, 1)
            dve.wait_ge(s_kc, 1)

            def one_hots(u, first_window, nw):
                for buf, keys in ((Lb[u], src_lo), (Rb[u], key)):
                    m = buf.shape[1]
                    k_ = keys[:, bass.ds(first_window, nw)].rearrange("p (o w) -> p o w", o=1).broadcast_to((128, m, nw))
                    last_ = V.tensor_tensor(buf[:, :, 0:nw], count12[:, 0:m, 0:nw], k_, ALU.is_equal)
                return last_

            with dve.Fori(0, BATCHES // 2) as i:
                for u in range(2):
                    dve.wait_ge(s_mm[u], i + OPEN)
                    one_hots(u, (i * 2 + u) * BATCH, BATCH).then_inc(s_lr[u], 1)
            dve.wait_ge(s_mm[0], BATCHES // 2 + OPEN)
            one_hots(0, WINDOWS - 1, 1).then_inc(s_last[0], 1)

            missed = dve.value_load(flag[0:1, 0:1], min_val=0, max_val=1)
            with dve.If(missed != 0):
                dve.wait_ge(s_last[2], 1)
                dve.wait_ge(g_in, 32)
                dve.wait_ge(g_count, 1)
                V.tensor_copy(e_dst, e_raw.bitcast(I32))
                V.tensor_copy(e_src, e_sk.bitcast(I32))
                V.memset(g_one, 1.0)
                V.memset(g_zero, 0.0).then_inc(g_conv, 1)
                dve.wait_ge(g_conv, 1)

                def turns(j, number, with_left):
                    first_turn = (j * (TILES + 1) + number) * TURNS
                    with dve.Fori(0, TURNS) as c:
                        dve.wait_ge(g_conv, j * per_block + number + 2)
                        dve.wait_ge(g_done, first_turn + c + OPEN)
                        for s in range(SUB):
                            at_ = bass.ds(c * SUB + s, 1)
                            if with_left:
                                V.tensor_scalar(gL[:, s, :], c625[:, 0:128], e_sk[:, at_], None, ALU.is_equal)
                            last_ = V.tensor_scalar(gR[:, s, :], c625, e_dst[:, at_], None, ALU.is_equal)
                        last_.then_inc(g_ready, 1)
                    dve.wait_ge(g_tile, j * (TILES + 1) + number + 1)

                per_block = TILES + 2
                with dve.Fori(0, 5) as j:
                    V.tensor_copy(e_sk, e_src).then_inc(g_conv, 1)
                    with dve.Fori(0, TILES) as k:
                        turns(j, k, True)
                        dve.wait_ge(g_store, (j * TILES + k + OPEN) * 16)
                        for b, (c0, n_) in enumerate(HALVES):
                            last = V.tensor_copy(g_rest[:, c0:c0 + n_], ps[0:P, b, 0:n_])
                        last.then_inc(g_restk, 1)
                        dve.wait_ge(g_restk, j * TILES + k + 1)
                        for b, (c0, n_) in enumerate(HALVES):
                            last = V.tensor_tensor(
                                adj[:, bass.ds(k, 1), bass.ds(j * BLOCK + c0, n_)].rearrange("p k d -> p (k d)"),
                                ps[0:P, b, 0:n_], g_rest[:, c0:c0 + n_], ALU.subtract)
                        last.then_inc(g_kept, 1)
                        V.tensor_scalar(e_sk, e_sk, -float(P), None, ALU.add).then_inc(g_conv, 1)
                    turns(j, TILES, False)
                    dve.wait_ge(g_degs, (j + OPEN) * 16)
                    for b, (c0, n_) in enumerate(HALVES):
                        last = V.tensor_copy(g_deg[:, c0:c0 + n_], ps[0:1, b, 0:n_])
                    last.then_inc(g_degk, 1)
                    V.tensor_scalar(e_dst, e_dst, -float(BLOCK), None, ALU.add).then_inc(g_conv, 1)
                dve.wait_ge(g_degl, 16)

            V.tensor_scalar(root[0:P, :], deg[0:P, :], 1.0, None, ALU.add).then_inc(s_deg1, 1)
            link(V.tensor_scalar(rdeg[0:P, :], deg[0:P, :], 1.0, None, ALU.max))
            link(V.reciprocal(rdeg[0:P, :], rdeg[0:P, :]))
            dve.wait_ge(s_sqrt, 1)
            V.reciprocal(dinv[0:P, :], root[0:P, :]).then_inc(s_norms, 1)
            dve.wait_ge(s_norms_in, 32)

            with dve.Fori(0, STEPS) as t:
                def means(g):
                    k0, nt = GROUPS[g]
                    n_ = nt * P
                    dve.wait_ge(s_agg, t * NG + g + 1)
                    dve.wait_ge(s_hid, t * 2 * NG + (2 * g if g < TAIL else 0) + OPEN)
                    V.tensor_tensor(agg[g == TAIL][:, 0:n_], ps_agg[2 if g == TAIL else g % 2][:, 0:n_],
                                    row[:, k0 * P:k0 * P + n_], ALU.mult).then_inc(s_aggT, 1)

                def add_bias(g):
                    nt = GROUPS[g][1]
                    dve.wait_ge(s_out, t * NG + g + 1 + OPEN)
                    p_ = ps_out[g == TAIL][0:P, 0:nt * FEAT].rearrange("p (k f) -> p k f", f=FEAT)
                    V.tensor_tensor(p_, p_, bias_of(1, nt), ALU.add).then_inc(s_bias, 1)

                def update(g):
                    n_ = GROUPS[g][1] * FEAT
                    dve.wait_ge(s_tanh, t * NG + g + 1 + OPEN)
                    V.scalar_tensor_tensor(out=tiles_of(state, g), in0=tiles_of(state, g), scalar=keep[0:P, :],
                                           in1=act_out[:, 0:n_], op0=ALU.mult, op1=ALU.add).then_inc(s_upd, 1)

                def next_lo(g):
                    split_lo(g, (t + 1) * NG + g + 1, next_scale[0:P, :])

                dve.wait_ge(s_hi, (t + 1) * NG)
                dve.wait_ge(s_lo, (t + 1) * NG)
                V.tensor_scalar(now_unscale, unscale[:, bass.ds(t, 1)], 1.0, None, ALU.mult)
                V.tensor_scalar(next_scale, scale[:, bass.ds(t + 1, 1)], 1.0, None, ALU.mult).then_inc(s_now, 1)

                for g in range(TAIL):
                    if g >= 2:
                        add_bias(g - 2)
                        update(g - 2)
                    means(g)
                means(TAIL)
                add_bias(TAIL - 2)
                update(TAIL - 2)
                dve.wait_ge(s_now, t + 1)
                for g in range(3):
                    next_lo(g)
                add_bias(TAIL - 1)
                update(TAIL - 1)
                for g in range(3, TAIL - 1):
                    next_lo(g)
                add_bias(TAIL)
                update(TAIL)
                for g in range(TAIL - 1, NG):
                    next_lo(g)

            aflat = adj_flat
            step = NODES + P
            diag = aflat[:, 0:(TILES - 1) * step].rearrange("p (k r) -> p k r", r=step)[:, :, 0:P]
            V.tensor_tensor(diag, diag, ident[:, :].rearrange("p (o d) -> p o d", o=1).broadcast_to((P, TILES - 1, P)),
                            ALU.add)
            corner = aflat[:, (TILES - 1) * step:(TILES - 1) * step + P]
            V.tensor_tensor(corner, corner, ident[:, :], ALU.add).then_inc(s_diag, 1)

            dve.wait_ge(s_upd, (STEPS + 1) * NG)
            for g in range(NG):
                dve.wait_ge(s_xr[g], 16)
                V.scalar_tensor_tensor(out=tiles_of(state, g), in0=tiles_of(state, g), scalar=DT,
                                       in1=tiles_of(xload, g), op0=ALU.mult, op1=ALU.add).then_inc(s_x2, 1)
            dve.wait_ge(s_x2, NG)
            statistics(lambda g: None).then_inc(s_x2v, 1)
            dve.wait_ge(s_x2s, 1)
            link(V.reciprocal(ln_a[0:P, :], ln_a[0:P, :]))
            link(V.scalar_tensor_tensor(out=ln_a[0:P, :], in0=ln_a[0:P, :], scalar=LN_SCALE, in1=dinv_col[0:P, :],
                                        op0=ALU.mult, op1=ALU.mult))
            link(V.scalar_tensor_tensor(out=ln_b[0:P, :], in0=mv[:, :, 0], scalar=-1.0, in1=ln_a[0:P, :],
                                        op0=ALU.mult, op1=ALU.mult))
            for g, (k0, nt) in enumerate(GROUPS):
                t_ = lnt[g % 2]
                n_ = nt * FEAT
                for i in range(nt):
                    k = k0 + i
                    last = V.tensor_scalar(t_[:, i * FEAT:(i + 1) * FEAT], state[:, k, :], ln_a[0:P, k:k + 1],
                                           ln_b[0:P, k:k + 1], ALU.mult, ALU.add)
                link(last)
                link(V.tensor_scalar(tiles_of(hi, g), t_[:, 0:n_], 0.0, None, ALU.max))
                V.scalar_tensor_tensor(out=tiles_of(lo, g), in0=t_[:, 0:n_], scalar=0.0, in1=tiles_of(hi, g),
                                       op0=ALU.max, op1=ALU.subtract).then_inc(c_lo[0], 1)

            for layer in range(2):
                def scaled(g):
                    k0, nt = GROUPS[g]
                    n_ = nt * P
                    dve.wait_ge(c_agg[layer], g + 1)
                    if 0 < g < TAIL:
                        dve.wait_ge(c_out[layer], g)
                    V.tensor_tensor(agg[g == TAIL][:, 0:n_], ps_agg[2 if g == TAIL else g % 2][:, 0:n_],
                                    row[:, k0 * P:k0 * P + n_], ALU.mult).then_inc(c_aggT[layer], 1)

                def rows_out(g):
                    k0, nt = GROUPS[g]
                    n_ = nt * FEAT
                    dve.wait_ge(c_out[layer], g + 1)
                    p_ = ps_out[g == TAIL][0:P, 0:n_].rearrange("p (k f) -> p k f", f=FEAT)
                    a_ = act_out[:, 0:n_].rearrange("p (k f) -> p k f", f=FEAT)
                    back = 1 / LN_SCALE if layer == 0 else top[0:P, 3:4]
                    ins = V.scalar_tensor_tensor(out=a_, in0=p_, scalar=back, in1=bias_of(2 + layer, nt),
                                                 op0=ALU.mult, op1=ALU.add)
                    if layer == 0:
                        ins.then_inc(c_use[0], 1)
                        dve.wait_ge(c_use[0], g + 1)
                        d_ = dinv_col[0:P, k0:k0 + nt].rearrange("p (k o) -> p k o", o=1).broadcast_to((P, nt, FEAT))
                        link(V.scalar_tensor_tensor(out=state[:, k0:k0 + nt, :], in0=a_, scalar=0.0, in1=d_,
                                                    op0=ALU.max, op1=ALU.mult))
                        V.tensor_reduce(part_max[0:P, g:g + 1], tiles_of(state, g), AX.X, ALU.max)
                    else:
                        link(ins)
                        V.tensor_tensor(tiles_of(state, g), tiles_of(state, g), act_out[:, 0:n_], ALU.add
                                        ).then_inc(c_use[1], 1)
                        dve.wait_ge(c_use[1], g + 1)

                if layer == 0:
                    dve.wait_ge(s_dinv, 16)
                    dve.wait_ge(s_x2o, 16)
                for g in range(NG):
                    scaled(g)
                    if g == 0 and layer == 1:
                        dve.wait_ge(s_x2i, 16)
                    if g >= 1:
                        rows_out(g - 1)
                rows_out(TAIL)

                if layer == 0:
                    link(V.memset(ones_row, 1.0))
                    V.tensor_reduce(part_max[0:P, 7:8], part_max[0:P, 0:NG], AX.X, ALU.max).then_inc(s_mx, 1)
                    dve.wait_ge(s_mxT, 1)
                    V.tensor_reduce(top[0:1, 0:1], ps[0:1, 7, 0:P], AX.X, ALU.max).then_inc(s_mx, 1)
                    dve.wait_ge(s_mxT, 2)
                    link(V.tensor_scalar(top[:, 0:1], ps[:, 7, 128:129], 2.0**-100, None, ALU.max))
                    power_of_two(top[:, 1:2], top[:, 2:3], top[:, 0:1])
                    link(V.tensor_scalar(top[:, 3:4], top[:, 1:2], 2.0**-SPLIT_TOP, None, ALU.mult))
                    V.tensor_scalar(top[:, 2:3], top[:, 2:3], 2.0**SPLIT_TOP, None, ALU.mult).then_inc(s_top, 1)
                    dve.wait_ge(s_top, 1)
                    for g in range(NG):
                        dve.wait_ge(c_hi, g + 1)
                        V.scalar_tensor_tensor(out=tiles_of(lo, g), in0=tiles_of(state, g), scalar=top[0:P, 2:3],
                                               in1=tiles_of(hi, g), op0=ALU.mult, op1=ALU.subtract
                                               ).then_inc(c_lo[1], 1)


_INS = ["x", "src", "dst", "L0_gnn_W_in", "L0_gnn_b_in", "L0_gnn_W1", "L0_gnn_b1", "L0_gnn_W2", "L0_gnn_b2",
        "L0_gnn_clearance", "L1_gnn_W1", "L1_gnn_b1", "L1_gnn_W2", "L1_gnn_b2"]
_OUTS = [((NODES, FEAT), "float32")]


def kernel(**inputs):
    import numpy as _np
    import concourse.bacc as _bacc
    from concourse import mybir as _mybir
    from concourse.bass_utils import run_bass_kernel_spmd as _run

    nc = _bacc.Bacc("TRN2", target_bir_lowering=False, num_devices=1)
    arrays, args = {}, []
    for name in _INS:
        a = _np.ascontiguousarray(inputs[name])
        arrays[f"in_{name}_dram"] = a
        args.append(nc.dram_tensor(f"in_{name}_dram", a.shape, _mybir.dt.from_np(a.dtype), kind="ExternalInput").ap())
    for i, (shape, dtype) in enumerate(_OUTS):
        dt = _mybir.dt.from_np(_np.dtype(dtype))
        args.append(nc.dram_tensor(f"out_{i}_dram", shape, dt, kind="ExternalOutput").ap())
    gnn_kernel(nc, *args)
    r = _run(nc, [arrays], core_ids=[0])
    got = tuple(r.results[0][f"out_{i}_dram"] for i in range(len(_OUTS)))
    return got[0]
```
